# Optimizing a Trainium2 kernel written in Bass

```python
import numpy as np
import jax
import jax.numpy as jnp

def _softmax(x, axis=-1):
    return jax.nn.softmax(x, axis=axis)

def _gelu(x):
    return jax.nn.gelu(x, approximate=True)

def _silu(x):
    return jax.nn.silu(x)

def _sigmoid(x):
    return jax.nn.sigmoid(x)

def _layernorm(x, axis=-1, eps=1e-05):
    m = jnp.mean(x, axis=axis, keepdims=True)
    v = jnp.var(x, axis=axis, keepdims=True)
    return (x - m) / jnp.sqrt(v + eps)

def _scatter_add(tgt, idx, src, axis=0):
    return tgt.at[idx].add(src)

def _segment_sum(src, seg, n):
    return jax.ops.segment_sum(src, seg, n)
kernel_name = 'mk_dlrm_tower_d1_rec_r8_b0b5d6'

def setup_inputs(seed: int=0):
    np.random.seed(seed)
    _w = jnp.asarray

    def _rec_inputs():
        import jax
        import jax.numpy as jnp
        _tk = jax.random.key(seed)
        dense_ctx = jax.random.normal(jax.random.fold_in(_tk, 190), (2048, 16), jnp.float32)
        ids = jnp.stack([jax.random.randint(jax.random.fold_in(_tk, 200 + f), (2048,), 0, v, jnp.int32) for f, v in enumerate([1250, 125000, 12500, 1000, 1250, 1000, 1250, 1250, 1250, 1250, 12500, 1250, 1250, 1250, 12500, 12500, 12500, 1000, 12500, 12500, 1250, 1000, 12500, 1250, 1000, 1250, 1250])], axis=1)
        tbl_0 = 0.05 * jax.random.normal(jax.random.fold_in(_tk, 500 + 0), (1250, 128), jnp.float32)
        tbl_1 = 0.05 * jax.random.normal(jax.random.fold_in(_tk, 500 + 1), (125000, 128), jnp.float32)
        tbl_2 = 0.05 * jax.random.normal(jax.random.fold_in(_tk, 500 + 2), (12500, 128), jnp.float32)
        tbl_3 = 0.05 * jax.random.normal(jax.random.fold_in(_tk, 500 + 3), (1000, 128), jnp.float32)
        tbl_4 = 0.05 * jax.random.normal(jax.random.fold_in(_tk, 500 + 4), (1250, 128), jnp.float32)
        tbl_5 = 0.05 * jax.random.normal(jax.random.fold_in(_tk, 500 + 5), (1000, 128), jnp.float32)
        tbl_6 = 0.05 * jax.random.normal(jax.random.fold_in(_tk, 500 + 6), (1250, 128), jnp.float32)
        tbl_7 = 0.05 * jax.random.normal(jax.random.fold_in(_tk, 500 + 7), (1250, 128), jnp.float32)
        tbl_8 = 0.05 * jax.random.normal(jax.random.fold_in(_tk, 500 + 8), (1250, 128), jnp.float32)
        tbl_9 = 0.05 * jax.random.normal(jax.random.fold_in(_tk, 500 + 9), (1250, 128), jnp.float32)
        tbl_10 = 0.05 * jax.random.normal(jax.random.fold_in(_tk, 500 + 10), (12500, 128), jnp.float32)
        tbl_11 = 0.05 * jax.random.normal(jax.random.fold_in(_tk, 500 + 11), (1250, 128), jnp.float32)
        tbl_12 = 0.05 * jax.random.normal(jax.random.fold_in(_tk, 500 + 12), (1250, 128), jnp.float32)
        tbl_13 = 0.05 * jax.random.normal(jax.random.fold_in(_tk, 500 + 13), (1250, 128), jnp.float32)
        tbl_14 = 0.05 * jax.random.normal(jax.random.fold_in(_tk, 500 + 14), (12500, 128), jnp.float32)
        tbl_15 = 0.05 * jax.random.normal(jax.random.fold_in(_tk, 500 + 15), (12500, 128), jnp.float32)
        tbl_16 = 0.05 * jax.random.normal(jax.random.fold_in(_tk, 500 + 16), (12500, 128), jnp.float32)
        tbl_17 = 0.05 * jax.random.normal(jax.random.fold_in(_tk, 500 + 17), (1000, 128), jnp.float32)
        tbl_18 = 0.05 * jax.random.normal(jax.random.fold_in(_tk, 500 + 18), (12500, 128), jnp.float32)
        tbl_19 = 0.05 * jax.random.normal(jax.random.fold_in(_tk, 500 + 19), (12500, 128), jnp.float32)
        tbl_20 = 0.05 * jax.random.normal(jax.random.fold_in(_tk, 500 + 20), (1250, 128), jnp.float32)
        tbl_21 = 0.05 * jax.random.normal(jax.random.fold_in(_tk, 500 + 21), (1000, 128), jnp.float32)
        tbl_22 = 0.05 * jax.random.normal(jax.random.fold_in(_tk, 500 + 22), (12500, 128), jnp.float32)
        tbl_23 = 0.05 * jax.random.normal(jax.random.fold_in(_tk, 500 + 23), (1250, 128), jnp.float32)
        tbl_24 = 0.05 * jax.random.normal(jax.random.fold_in(_tk, 500 + 24), (1000, 128), jnp.float32)
        tbl_25 = 0.05 * jax.random.normal(jax.random.fold_in(_tk, 500 + 25), (1250, 128), jnp.float32)
        tbl_26 = 0.05 * jax.random.normal(jax.random.fold_in(_tk, 500 + 26), (1250, 128), jnp.float32)
        _rk = jax.random.fold_in(_tk, 7)
        W_top1 = 0.0521996 * jax.random.normal(jax.random.fold_in(_tk, 801), (367, 512), jnp.float32)
        W_top2 = 0.0441942 * jax.random.normal(jax.random.fold_in(_tk, 802), (512, 256), jnp.float32)
        W_top3 = 0.0625 * jax.random.normal(jax.random.fold_in(_tk, 803), (256, 1), jnp.float32)
        b_top1 = jnp.zeros((512,), jnp.float32)
        b_top2 = jnp.zeros((256,), jnp.float32)
        return (dense_ctx, ids, tbl_0, tbl_1, tbl_2, tbl_3, tbl_4, tbl_5, tbl_6, tbl_7, tbl_8, tbl_9, tbl_10, tbl_11, tbl_12, tbl_13, tbl_14, tbl_15, tbl_16, tbl_17, tbl_18, tbl_19, tbl_20, tbl_21, tbl_22, tbl_23, tbl_24, tbl_25, tbl_26, W_top1, b_top1, W_top2, b_top2, W_top3)
    dense_ctx, ids, tbl_0, tbl_1, tbl_2, tbl_3, tbl_4, tbl_5, tbl_6, tbl_7, tbl_8, tbl_9, tbl_10, tbl_11, tbl_12, tbl_13, tbl_14, tbl_15, tbl_16, tbl_17, tbl_18, tbl_19, tbl_20, tbl_21, tbl_22, tbl_23, tbl_24, tbl_25, tbl_26, W_top1, b_top1, W_top2, b_top2, W_top3 = _rec_inputs()

    def _L0_rec_setup():
        import jax, jax.numpy as jnp
        import numpy as np
        B, F, D = (2048, 27, 128)
        _TRIL_I, _TRIL_J = np.tril_indices(F, k=-1)
        key = jax.random.key(seed)
        features = jax.random.normal(key, (B, F, D), dtype=jnp.float32)
        return {'features': features}
    _L0_rec_all = _L0_rec_setup()
    _L0_rec_in = {k: v for k, v in _L0_rec_all.items() if k in ()}
    del _L0_rec_all
    return {'dense_ctx': dense_ctx, 'ids': ids, 'tbl_0': tbl_0, 'tbl_1': tbl_1, 'tbl_2': tbl_2, 'tbl_3': tbl_3, 'tbl_4': tbl_4, 'tbl_5': tbl_5, 'tbl_6': tbl_6, 'tbl_7': tbl_7, 'tbl_8': tbl_8, 'tbl_9': tbl_9, 'tbl_10': tbl_10, 'tbl_11': tbl_11, 'tbl_12': tbl_12, 'tbl_13': tbl_13, 'tbl_14': tbl_14, 'tbl_15': tbl_15, 'tbl_16': tbl_16, 'tbl_17': tbl_17, 'tbl_18': tbl_18, 'tbl_19': tbl_19, 'tbl_20': tbl_20, 'tbl_21': tbl_21, 'tbl_22': tbl_22, 'tbl_23': tbl_23, 'tbl_24': tbl_24, 'tbl_25': tbl_25, 'tbl_26': tbl_26, 'W_top1': W_top1, 'b_top1': b_top1, 'W_top2': W_top2, 'b_top2': b_top2, 'W_top3': W_top3}

def reference(dense_ctx, ids, tbl_0, tbl_1, tbl_2, tbl_3, tbl_4, tbl_5, tbl_6, tbl_7, tbl_8, tbl_9, tbl_10, tbl_11, tbl_12, tbl_13, tbl_14, tbl_15, tbl_16, tbl_17, tbl_18, tbl_19, tbl_20, tbl_21, tbl_22, tbl_23, tbl_24, tbl_25, tbl_26, W_top1, b_top1, W_top2, b_top2, W_top3):
    import jax
    import jax.numpy as jnp

    def _L0_rec_ref(features):
        import jax, jax.numpy as jnp
        import numpy as np
        B, F, D = (2048, 27, 128)
        _TRIL_I, _TRIL_J = np.tril_indices(F, k=-1)
        xactions = jnp.einsum('bfd,bgd->bfg', features, features)
        activations = xactions[:, _TRIL_I, _TRIL_J]
        return activations
    e = jnp.stack([tbl_0[ids[:, 0]], tbl_1[ids[:, 1]], tbl_2[ids[:, 2]], tbl_3[ids[:, 3]], tbl_4[ids[:, 4]], tbl_5[ids[:, 5]], tbl_6[ids[:, 6]], tbl_7[ids[:, 7]], tbl_8[ids[:, 8]], tbl_9[ids[:, 9]], tbl_10[ids[:, 10]], tbl_11[ids[:, 11]], tbl_12[ids[:, 12]], tbl_13[ids[:, 13]], tbl_14[ids[:, 14]], tbl_15[ids[:, 15]], tbl_16[ids[:, 16]], tbl_17[ids[:, 17]], tbl_18[ids[:, 18]], tbl_19[ids[:, 19]], tbl_20[ids[:, 20]], tbl_21[ids[:, 21]], tbl_22[ids[:, 22]], tbl_23[ids[:, 23]], tbl_24[ids[:, 24]], tbl_25[ids[:, 25]], tbl_26[ids[:, 26]]], axis=1)
    z = _L0_rec_ref(e)
    z = z.reshape(z.shape[0], -1)
    h = jnp.concatenate([z, dense_ctx], axis=1)
    h = jnp.maximum(h @ W_top1 + b_top1, 0.0)
    h = jnp.maximum(h @ W_top2 + b_top2, 0.0)
    y = h @ W_top3
    return y

_drawn_inputs = setup_inputs


def setup_inputs(seed=0):
    import zlib

    import numpy as np

    out = dict(_drawn_inputs(seed))
    spreads = {'b_top1': (0.0, 0.1), 'b_top2': (0.0, 0.1)}
    factors = {}
    for name, (base, spread) in spreads.items():
        noise = np.random.default_rng([zlib.crc32(name.encode()), seed]).standard_normal(out[name].shape)
        drawn = base * np.exp(spread * noise) if base else spread * noise
        out[name] = jnp.asarray(drawn.astype(out[name].dtype))
    for name, factor in factors.items():
        out[name] = (out[name] * factor).astype(out[name].dtype)
    return out
```

```python
from contextlib import ExitStack

import numpy as np

import concourse.bass as bass
from concourse import mybir

F32 = mybir.dt.float32
F32R = mybir.dt.float32r
I32 = mybir.dt.int32
U32 = mybir.dt.uint32
ALU = mybir.AluOpType
ACT = mybir.ActivationFunctionType

P = 128
BATCH = 2048
FEATURES = 27
DIM = 128
DENSE = 16
VOCAB = [1250, 125000, 12500, 1000, 1250, 1000, 1250, 1250, 1250, 1250, 12500, 1250, 1250, 1250,
         12500, 12500, 12500, 1000, 12500, 12500, 1250, 1000, 12500, 1250, 1000, 1250, 1250]
HIDDEN1, HIDDEN2 = 512, 256

N_HOT = 8
HOT = sorted(range(FEATURES), key=lambda f: (VOCAB[f], f))[:N_HOT]
COLD = [f for f in range(FEATURES) if f not in HOT]
N_COLD = len(COLD)
ORDER = COLD + HOT
HOT_ROWS = 125
HOT_CHUNKS = [VOCAB[f] // HOT_ROWS for f in HOT]
MAX_CHUNKS = max(HOT_CHUNKS)
CHUNK_AT = [sum(HOT_CHUNKS[:k]) for k in range(N_HOT)]
ALL_CHUNKS = sum(HOT_CHUNKS)

TILES = BATCH // P
GROUP_TILES = 2
COLS = GROUP_TILES * P
GROUPS = TILES // GROUP_TILES
ROW_RING = 4
HOT_RING = 2

STRIPS = 4
STRIP = COLS // STRIPS
PAIR_COLS = FEATURES - 1
BANK_ROWS = 16
PAIR_BANKS = STRIP // BANK_ROWS

PAIRS = FEATURES * (FEATURES - 1) // 2
IN1 = PAIRS + DENSE
K1 = [P, P, IN1 - 2 * P]
K2 = HIDDEN1 // P
M2 = HIDDEN2 // P

COLD_FILLS = [(t, c, min(4, N_COLD - c)) for t in range(GROUP_TILES) for c in range(0, N_COLD, 4)]
HOT_FILLS = [(k, min(2, N_HOT - k)) for k in range(0, N_HOT, 2)]
N_CF, N_HF = len(COLD_FILLS), len(HOT_FILLS)
TILE_CF = N_CF // GROUP_TILES
FILLS = N_CF + N_HF
FILL_RING = 4 if (2 * FILLS) % 4 == 0 else 3 if (2 * FILLS) % 3 == 0 else 2
LAYER1_AFTER, LAYER2_AFTER = N_HF - 2, N_HF - 1


def pair_pieces():
    for i in range(1, FEATURES):
        at, j = i * (i - 1) // 2, 0
        while j < i:
            n = min(i - j, P - (at + j) % P)
            yield i, j, n, (at + j) // P, (at + j) % P
            j += n


PIECES = list(pair_pieces())
MOVES = 2 * len(PIECES) + 1


def row_order():
    rows = []
    for i in range(1, FEATURES):
        for j in range(i):
            hi, lo = max(ORDER[i], ORDER[j]), min(ORDER[i], ORDER[j])
            rows.append(hi * (hi - 1) // 2 + lo)
    return rows + list(range(PAIRS, IN1))


def wait_count(engine, semaphore, count):
    if not isinstance(count, int) or count > 0:
        engine.wait_ge(semaphore, count)


def build(nc, ids, ids_hot, tables, dense, w1, w2, vectors_dram, out):
    with ExitStack() as ctx:
        def sb(name, shape, dtype=F32):
            return ctx.enter_context(nc.sbuf_tensor(name, shape, dtype))

        def sem(name):
            return ctx.enter_context(nc.semaphore(name))

        ids_sb = sb("ids_sb", [P, TILES * FEATURES], I32)
        index = sb("index", [P, ROW_RING, FEATURES], I32)
        rows = sb("rows", [P, ROW_RING, N_COLD, DIM])
        hot_ids = sb("hot_ids", [P, N_HOT, COLS], I32)
        table_hi = sb("table_hi", [P, ALL_CHUNKS, DIM], F32R)
        table_lo = sb("table_lo", [P, ALL_CHUNKS, DIM], F32R)
        one_hot = sb("one_hot", [P, HOT_RING, MAX_CHUNKS, COLS], F32R)
        row_id_int = sb("row_id_int", [P, 2, MAX_CHUNKS], I32)
        row_id = sb("row_id", [P, 2, MAX_CHUNKS])
        ident = sb("ident", [P, P])
        et = sb("et", [P, COLS, FEATURES])
        pairs = sb("pairs", [P, PAIR_COLS, P])
        zt = sb("zt", [P, len(K1), COLS])
        w1_sb = sb("w1_sb", [P, len(K1), HIDDEN1])
        w2_sb = sb("w2_sb", [P, K2, HIDDEN2])
        vectors = sb("vectors", [P, K2 + 2 * M2])
        b1_sb, b2_sb, w3_sb = vectors[:, 0:K2], vectors[:, K2:K2 + M2], vectors[:, K2 + M2:K2 + 2 * M2]
        h1 = sb("h1", [P, K2, COLS])
        h2 = sb("h2", [P, M2, COLS])
        y_sb = sb("y_sb", [P, TILES])
        raw_all = pairs[:, :, :].rearrange("p a b -> p (a b)")
        raw = [raw_all[:, s * MAX_CHUNKS * DIM:(s + 1) * MAX_CHUNKS * DIM] for s in range(2)]

        fill_ps = [ctx.enter_context(nc.psum_tensor(f"fill_ps{i}", [P, 512], F32)) for i in range(FILL_RING)]
        pair_ps = [ctx.enter_context(nc.psum_tensor(f"pair_ps{i}", [P, 512], F32)) for i in range(2)]
        mlp_ps = [ctx.enter_context(nc.psum_tensor(f"mlp_ps{i}", [P, 512], F32)) for i in range(2)]

        ids_in = sem("ids_in")
        index_ok = sem("index_ok")
        rows_in = [sem(f"rows_in{s}") for s in range(ROW_RING)]
        gather_tick = sem("gather_tick")
        hot_ids_in = [sem(f"hot_ids_in{k}") for k in range(N_HOT)]
        raw_in = [sem(f"raw_in{s}") for s in range(2)]
        hi_made = sem("hi_made")
        lo_made = sem("lo_made")
        hot_made = sem("hot_made")
        hot_used = sem("hot_used")
        consts = sem("consts")
        row_id_ok = sem("row_id_ok")
        cold_full = sem("cold_full")
        fill_moved = sem("fill_moved")
        pair_full = sem("pair_full")
        pair_moved_v = sem("pair_moved_v")
        pair_moved_a = sem("pair_moved_a")
        z_in = sem("z_in")
        w_in = sem("w_in")
        h1_full = sem("h1_full")
        h1_done = sem("h1_done")
        h2_full = sem("h2_full")
        h2_done = sem("h2_done")
        y_full = sem("y_full")
        y_done = sem("y_done")
        stored = sem("stored")

        N_W = len(K1) + 2
        block = ctx.enter_context(nc.Block())

        def periods(engine, period):
            period(0, 0)
            period(0, 1)
            with engine.Fori(1, GROUPS // 2) as turn:
                period(turn, 0)
                period(turn, 1)

        def is_first(turn, h):
            return isinstance(turn, int) and turn == 0 and h == 0

        def mlp_psum(m):
            return mlp_ps[m // 2][:, (m % 2) * COLS:(m % 2 + 1) * COLS]

        def load_hot_ids(engine, i):
            for k in range(N_HOT):
                engine.dma_start(hot_ids[0:HOT_ROWS, k, :],
                                 ids_hot[k:k + 1, bass.ds(i * COLS, COLS)].to_broadcast([HOT_ROWS, COLS])
                                 ).then_inc(hot_ids_in[k], 16)

        def move_pairs(engine, i, half, moved, copy):
            for bank in range(PAIR_BANKS):
                engine.wait_ge(pair_full, i * PAIR_BANKS + bank + 1)
                for b in range(2):
                    s = 2 * half + b
                    frm = pair_ps[bank % 2][32 * s:32 * s + PAIR_COLS, 0:BANK_ROWS * PAIR_COLS].rearrange(
                        "p (r g) -> p g r", r=BANK_ROWS)
                    at = b * STRIP + bank * BANK_ROWS
                    last = copy(pairs[32 * half:32 * half + PAIR_COLS, :, at:at + BANK_ROWS], frm)
                last.then_inc(moved, 1)

        @block.sync
        def _(sp):
            sp.dma_start(ids_sb[:, :], ids.rearrange("(p t) f -> p (t f)", t=TILES)).then_inc(ids_in, 16)
            for k, f in enumerate(HOT):
                wait_count(sp, lo_made, k - 1)
                sp.dma_start(raw[k % 2][0:HOT_ROWS, 0:HOT_CHUNKS[k] * DIM],
                             tables[f].rearrange("(p c) d -> p (c d)", p=HOT_ROWS)).then_inc(raw_in[k % 2], 16)

            def period(turn, h):
                i = 2 * turn + h
                wait_count(sp, h1_full, i)
                sp.dma_start(zt[K1[2] - DENSE:K1[2], 2, :], dense[:, bass.ds(i * COLS, COLS)]).then_inc(z_in, 16)
                sp.wait_ge(pair_moved_v, (i + 1) * PAIR_BANKS)
                sp.wait_ge(pair_moved_a, (i + 1) * PAIR_BANKS)
                for a, j, n, c, row in PIECES:
                    for half in range(2):
                        sp.dma_start(zt[row:row + n, c, half * P:(half + 1) * P],
                                     pairs[32 * half + j:32 * half + j + n, a - 1, :]).then_inc(z_in, 16)

            periods(sp, period)
            sp.wait_ge(y_done, GROUPS)
            sp.dma_start(out.rearrange("(p t) o -> p (t o)", t=TILES), y_sb[:, :]).then_inc(stored, 16)
            sp.wait_ge(stored, 16)

        @block.gpsimd
        def _(pool):
            nc.gpsimd.memset(ident[:, :], 0.0).then_inc(consts, 1)
            nc.gpsimd.iota(row_id_int[:, 0, :], pattern=[[1, MAX_CHUNKS]], base=0,
                           channel_multiplier=min(HOT_CHUNKS)).then_inc(consts, 1)
            nc.gpsimd.iota(row_id_int[:, 1, :], pattern=[[1, MAX_CHUNKS]], base=0,
                           channel_multiplier=MAX_CHUNKS).then_inc(consts, 1)
            pool.wait_ge(consts, 3)
            nc.gpsimd.affine_select(out=ident[:, :], in_=ident[:, :], compare_op=ALU.not_equal, fill=1.0, base=0,
                                    pattern=[[-1, P]], channel_multiplier=1).then_inc(consts, 1)
            pool.wait_ge(ids_in, 16)

            def period(turn, h):
                for t in range(GROUP_TILES):
                    s = h * GROUP_TILES + t
                    tile = turn * ROW_RING + s
                    if not isinstance(turn, int):
                        pool.wait_ge(cold_full, (tile - ROW_RING + 1) * TILE_CF)
                        pool.sem_inc(gather_tick, 1)
                    nc.gpsimd.tensor_copy(index[:, s, :], ids_sb[:, bass.ds(tile * FEATURES, FEATURES)]
                                          ).then_inc(index_ok, 1)
                    pool.wait_ge(index_ok, tile + 1)
                    if not isinstance(turn, int):
                        pool.sem_inc(gather_tick, 1)
                    for c, f in enumerate(COLD):
                        nc.gpsimd.indirect_dma_start(
                            out=rows[:, s, c, :], out_offset=None, in_=tables[f],
                            in_offset=bass.IndirectOffsetOnAxis(ap=index[:, s, f:f + 1].bitcast(U32), axis=0),
                        ).then_inc(rows_in[s], 16)

            periods(pool, period)

        @block.tensor
        def _(pe):
            def fill_bank(turn, h, n):
                wait_count(pe, fill_moved, (2 * turn + h) * FILLS + n + 1 - FILL_RING)
                return fill_ps[(h * FILLS + n) % FILL_RING]

            def transposes(turn, h, n0):
                for j, (t, c0, n) in enumerate(COLD_FILLS):
                    s = h * GROUP_TILES + t
                    if c0 == 0:
                        pe.wait_ge(rows_in[s], (turn + 1) * (16 * N_COLD))
                    bank = fill_bank(turn, h, n0 + j)
                    for c in range(n):
                        last = nc.tensor.transpose(bank[:, c * P:(c + 1) * P], rows[:, s, c0 + c, :], ident[:, :])
                    last.then_inc(cold_full, 1)

            def look_up(turn, h, n0, j):
                k0, n = HOT_FILLS[j]
                bank = fill_bank(turn, h, n0 + j)
                for k in range(k0, k0 + n):
                    if is_first(turn, h):
                        pe.wait_ge(hi_made, k + 1)
                        pe.wait_ge(lo_made, k + 1)
                    pe.wait_ge(hot_made, (2 * turn + h) * N_HOT + k + 1)
                    to = bank[:, (k - k0) * COLS:(k - k0 + 1) * COLS]
                    for c in range(HOT_CHUNKS[k]):
                        hot = one_hot[0:HOT_ROWS, (h * N_HOT + k) % HOT_RING, c, :]
                        nc.tensor.matmul(to, table_hi[0:HOT_ROWS, CHUNK_AT[k] + c, :], hot,
                                         start=(c == 0), stop=False)
                        last = nc.tensor.matmul(to, table_lo[0:HOT_ROWS, CHUNK_AT[k] + c, :], hot,
                                                start=False, stop=(c == HOT_CHUNKS[k] - 1))
                    last.then_inc(hot_used, 1)

            def layer1(i):
                pe.wait_ge(z_in, (i + 1) * (16 * MOVES))
                wait_count(pe, y_done, i)
                for m in range(K2):
                    for c, k in enumerate(K1):
                        last = nc.tensor.matmul(mlp_psum(m), w1_sb[0:k, c, m * P:(m + 1) * P], zt[0:k, c, :],
                                                start=(c == 0), stop=(c == len(K1) - 1))
                last.then_inc(h1_full, 1)

            def layer2(i):
                pe.wait_ge(h1_done, (i + 1) * K2)
                for m in range(M2):
                    for c in range(K2):
                        last = nc.tensor.matmul(mlp_psum(m), w2_sb[:, c, m * P:(m + 1) * P], h1[:, c, :],
                                                start=(c == 0), stop=(c == K2 - 1))
                last.then_inc(h2_full, 1)

            def layer3(i):
                pe.wait_ge(h2_done, (i + 1) * M2)
                for t in range(GROUP_TILES):
                    for c in range(M2):
                        last = nc.tensor.matmul(mlp_ps[1][:, t:t + 1], h2[:, c, t * P:(t + 1) * P],
                                                w3_sb[:, c:c + 1], start=(c == 0), stop=(c == M2 - 1))
                last.then_inc(y_full, 1)

            def all_pairs(i):
                pe.wait_ge(fill_moved, (i + 1) * FILLS)
                for bank in range(PAIR_BANKS):
                    wait_count(pe, pair_moved_v, i * PAIR_BANKS + bank - 1)
                    wait_count(pe, pair_moved_a, i * PAIR_BANKS + bank - 1)
                    for r in range(BANK_ROWS):
                        for strip in range(STRIPS):
                            row = strip * STRIP + bank * BANK_ROWS + r
                            last = nc.tensor.matmul(
                                pair_ps[bank % 2][32 * strip:32 * strip + PAIR_COLS, r * PAIR_COLS:(r + 1) * PAIR_COLS],
                                et[:, row, 0:FEATURES - 1], et[:, row, 1:FEATURES], start=True, stop=True)
                    last.then_inc(pair_full, 1)

            def period(turn, h):
                i = 2 * turn + h
                if is_first(turn, h):
                    for j in range(N_HF):
                        look_up(turn, h, 0, j)
                    transposes(turn, h, N_HF)
                else:
                    transposes(turn, h, 0)
                    for j in range(N_HF):
                        look_up(turn, h, N_CF, j)
                        if j == LAYER1_AFTER:
                            layer1(i - 1)
                        if j == LAYER2_AFTER:
                            layer2(i - 1)
                    layer3(i - 1)
                all_pairs(i)

            pe.wait_ge(consts, 4)
            pe.wait_ge(w_in, 16 * N_W)
            periods(pe, period)
            layer1(GROUPS - 1)
            layer2(GROUPS - 1)
            layer3(GROUPS - 1)

        @block.scalar
        def _(act):
            load_hot_ids(act, 0)
            for c, k in enumerate(K1):
                act.dma_start(w1_sb[0:k, c, :], w1[c * P:c * P + k, :]).then_inc(w_in, 16)
            act.dma_start(w2_sb[:, :, :], w2.rearrange("(c p) n -> p c n", p=P)).then_inc(w_in, 16)
            act.dma_start(vectors[:, :], vectors_dram).then_inc(w_in, 16)

            def bank(h, n):
                return fill_ps[(h * FILLS + n) % FILL_RING]

            def move_cold(turn, h, n0, j):
                t, c0, n = COLD_FILLS[j]
                act.wait_ge(cold_full, (2 * turn + h) * N_CF + j + 1)
                nc.scalar.copy(et[:, t * P:(t + 1) * P, c0:c0 + n].rearrange("p r f -> p f r"),
                               bank(h, n0 + j)[:, 0:n * P].rearrange("p (f r) -> p f r", f=n)).then_inc(fill_moved, 1)

            def move_hot(turn, h, n0, j):
                k0, n = HOT_FILLS[j]
                act.wait_ge(hot_used, (2 * turn + h) * N_HOT + k0 + n)
                f = N_COLD + k0
                nc.scalar.copy(et[:, :, f:f + n].rearrange("p r f -> p f r"),
                               bank(h, n0 + j)[:, 0:n * COLS].rearrange("p (f r) -> p f r", f=n)).then_inc(fill_moved, 1)

            def relu1(i):
                act.wait_ge(h1_full, i + 1)
                for m in range(K2):
                    nc.scalar.activation(h1[:, m, :], mlp_psum(m), ACT.Relu,
                                         bias=b1_sb[:, m:m + 1]).then_inc(h1_done, 1)

            def relu2(i):
                act.wait_ge(h2_full, i + 1)
                for m in range(M2):
                    nc.scalar.activation(h2[:, m, :], mlp_psum(m), ACT.Relu,
                                         bias=b2_sb[:, m:m + 1]).then_inc(h2_done, 1)

            def period(turn, h):
                i = 2 * turn + h
                if is_first(turn, h):
                    for j in range(N_HF):
                        move_hot(turn, h, 0, j)
                    for j in range(N_CF):
                        move_cold(turn, h, N_HF, j)
                else:
                    for j in range(N_CF):
                        move_cold(turn, h, 0, j)
                    for j in range(N_HF):
                        move_hot(turn, h, N_CF, j)
                        if j == LAYER1_AFTER:
                            relu1(i - 1)
                        if j == LAYER2_AFTER:
                            relu2(i - 1)
                act.wait_ge(hot_made, (i + 1) * N_HOT)
                load_hot_ids(act, i + 1)
                wait_count(act, z_in, i * (16 * MOVES))
                move_pairs(act, i, 1, pair_moved_a, nc.scalar.copy)

            act.wait_ge(w_in, 16 * N_W)
            periods(act, period)
            relu1(GROUPS - 1)
            relu2(GROUPS - 1)

        @block.vector
        def _(dve):
            dve.wait_ge(consts, 3)
            nc.vector.tensor_copy(row_id[:, :, :], row_id_int[:, :, :]).then_inc(row_id_ok, 1)
            dve.wait_ge(row_id_ok, 1)

            def cut_table(k):
                c0, c1 = CHUNK_AT[k], CHUNK_AT[k] + HOT_CHUNKS[k]
                dve.wait_ge(raw_in[k % 2], 16 * (k // 2 + 1))
                src = raw[k % 2][0:HOT_ROWS, 0:HOT_CHUNKS[k] * DIM].rearrange("p (c d) -> p c d", d=DIM)
                nc.vector.tensor_copy(table_hi[0:HOT_ROWS, c0:c1, :], src).then_inc(hi_made, 1)
                dve.wait_ge(hi_made, k + 1)
                nc.vector.tensor_tensor(table_lo[0:HOT_ROWS, c0:c1, :], src,
                                        table_hi[0:HOT_ROWS, c0:c1, :].bitcast(F32), ALU.subtract
                                        ).then_inc(lo_made, 1)

            def make_one_hot(turn, h, k):
                n = (2 * turn + h) * N_HOT + k
                dve.wait_ge(hot_ids_in[k], (2 * turn + h + 1) * 16)
                wait_count(dve, hot_used, n + 1 - HOT_RING)
                which = 0 if HOT_CHUNKS[k] == min(HOT_CHUNKS) else 1
                for c in range(HOT_CHUNKS[k]):
                    last = nc.vector.tensor_scalar(one_hot[0:HOT_ROWS, (h * N_HOT + k) % HOT_RING, c, :],
                                                   hot_ids[0:HOT_ROWS, k, :],
                                                   row_id[0:HOT_ROWS, which, c:c + 1], None, ALU.is_equal)
                last.then_inc(hot_made, 1)

            def output(i):
                dve.wait_ge(y_full, i + 1)
                nc.vector.tensor_scalar(y_sb[:, bass.ds(i * GROUP_TILES, GROUP_TILES)], mlp_ps[1][:, 0:GROUP_TILES],
                                        1.0, None, ALU.mult).then_inc(y_done, 1)

            def period(turn, h):
                i = 2 * turn + h
                for k in range(N_HOT):
                    if is_first(turn, h):
                        cut_table(k)
                    make_one_hot(turn, h, k)
                if not is_first(turn, h):
                    output(i - 1)
                wait_count(dve, z_in, i * (16 * MOVES))
                move_pairs(dve, i, 0, pair_moved_v, nc.vector.tensor_copy)

            periods(dve, period)
            output(GROUPS - 1)
            for k in range(N_HOT):
                dve.wait_ge(hot_ids_in[k], (GROUPS + 1) * 16)


def kernel(**inputs):
    import concourse.bacc as bacc
    from concourse.bass_utils import run_bass_kernel_spmd

    nc = bacc.Bacc("TRN2", target_bir_lowering=False, num_devices=1)
    arrays = {}

    def dram(name, array):
        array = np.ascontiguousarray(array)
        arrays[name] = array
        return nc.dram_tensor(name, array.shape, mybir.dt.from_np(array.dtype), kind="ExternalInput").ap()

    def by_tile(columns):
        n = columns.shape[1]
        return columns.reshape(P, TILES, n).transpose(2, 1, 0).reshape(n, BATCH)

    ids_np = np.asarray(inputs["ids"])
    hot_np = by_tile(ids_np[:, HOT])
    hot_np = np.concatenate([hot_np, hot_np[:, :COLS]], axis=1)
    ids = dram("ids_d", ids_np)
    ids_hot = dram("ids_hot_d", hot_np)
    tables = [dram(f"tbl_{f}_d", inputs[f"tbl_{f}"]) for f in range(FEATURES)]
    dense = dram("dense_d", by_tile(np.asarray(inputs["dense_ctx"])))
    w1 = dram("w1_d", np.asarray(inputs["W_top1"])[row_order()])
    w2 = dram("w2_d", inputs["W_top2"])
    vectors = dram("vectors_d", np.concatenate(
        [np.asarray(inputs[name]).reshape(-1, P).T for name in ("b_top1", "b_top2", "W_top3")], axis=1))
    out = nc.dram_tensor("out_d", (BATCH, 1), F32, kind="ExternalOutput").ap()
    build(nc, ids, ids_hot, tables, dense, w1, w2, vectors, out)
    result = run_bass_kernel_spmd(nc, [arrays], core_ids=[0])
    return result.results[0]["out_d"]
```

```python
from contextlib import ExitStack

import numpy as np

import concourse.bass as bass
from concourse import mybir

F32 = mybir.dt.float32
F32R = mybir.dt.float32r
I32 = mybir.dt.int32
U32 = mybir.dt.uint32
ALU = mybir.AluOpType
ACT = mybir.ActivationFunctionType

P = 128
BATCH = 2048
FEATURES = 27
DIM = 128
DENSE = 16
VOCAB = [1250, 125000, 12500, 1000, 1250, 1000, 1250, 1250, 1250, 1250, 12500, 1250, 1250, 1250,
         12500, 12500, 12500, 1000, 12500, 12500, 1250, 1000, 12500, 1250, 1000, 1250, 1250]
HIDDEN1, HIDDEN2 = 512, 256

N_HOT = 8
HOT = sorted(range(FEATURES), key=lambda f: (VOCAB[f], f))[:N_HOT]
COLD = [f for f in range(FEATURES) if f not in HOT]
N_COLD = len(COLD)
ORDER = COLD + HOT
HOT_ROWS = 125
HOT_CHUNKS = [VOCAB[f] // HOT_ROWS for f in HOT]
MAX_CHUNKS = max(HOT_CHUNKS)
CHUNK_AT = [sum(HOT_CHUNKS[:k]) for k in range(N_HOT)]
ALL_CHUNKS = sum(HOT_CHUNKS)

TILES = BATCH // P
GROUP_TILES = 2
COLS = GROUP_TILES * P
GROUPS = TILES // GROUP_TILES
HOT_RING = 2

STRIPS = 4
STRIP = COLS // STRIPS
PAIR_COLS = FEATURES - 1
BANK_ROWS = 16
PAIR_BANKS = STRIP // BANK_ROWS

TILE_FILLS = [(c, min(4, N_COLD - c)) for c in range(0, N_COLD, 4)]
HOT_FILLS = [(k, min(2, N_HOT - k)) for k in range(0, N_HOT, 2)]
N_TF, N_HF = len(TILE_FILLS), len(HOT_FILLS)
FILLS = GROUP_TILES * N_TF + N_HF
FILL_RING = 4 if (2 * FILLS) % 4 == 0 else 3 if (2 * FILLS) % 3 == 0 else 2

FIRST_ORDER = [("hot", j) for j in range(N_HF)] + [("tile", 0), ("tile", 1)]
ORDER_OF_STEPS = ([("hot", 0), ("hot", 1), ("tile", 0)] + [("hot", j) for j in range(2, N_HF - 1)]
                  + [("layer", 1), ("hot", N_HF - 1), ("layer", 2), ("tile", 1), ("layer", 3)])

PAIRS = FEATURES * (FEATURES - 1) // 2
HALF = PAIR_COLS // 2
SIDE = -(-(HALF + 1) // STRIPS)
K1 = [min(P, 32 * HALF + DENSE - c * P) for c in range(SIDE)]
K2 = HIDDEN1 // P
M2 = HIDDEN2 // P
MOVES = HALF + 1


def place(i):
    n = i - 1 if i <= HALF else i - 1 - HALF
    return n % STRIPS, n // STRIPS


def contraction_rows():
    def pair(i, j):
        hi, lo = max(ORDER[i], ORDER[j]), min(ORDER[i], ORDER[j])
        return hi * (hi - 1) // 2 + lo

    rows = [None] * (SIDE * P)
    for i in range(HALF + 1, FEATURES):
        strip, chunk = place(i)
        at, low = chunk * P + 32 * strip, FEATURES - i
        rows[at:at + FEATURES] = [pair(i, j) for j in range(i)] + [pair(low, j) for j in range(low)]
    rows[32 * HALF:32 * HALF + DENSE] = range(PAIRS, PAIRS + DENSE)
    return rows


def wait_count(engine, semaphore, count):
    if not isinstance(count, int) or count > 0:
        engine.wait_ge(semaphore, count)


def build(nc, ids, ids_hot, tables, dense, w1, w2, vectors_dram, out):
    with ExitStack() as ctx:
        def sb(name, shape, dtype=F32):
            return ctx.enter_context(nc.sbuf_tensor(name, shape, dtype))

        def sem(name):
            return ctx.enter_context(nc.semaphore(name))

        ids_sb = sb("ids_sb", [P, TILES * FEATURES], I32)
        index = sb("index", [P, GROUP_TILES, FEATURES], I32)
        rows = sb("rows", [P, GROUP_TILES, N_COLD, DIM])
        hot_ids = sb("hot_ids", [P, N_HOT, COLS], I32)
        table_hi = sb("table_hi", [P, ALL_CHUNKS, DIM], F32R)
        table_lo = sb("table_lo", [P, ALL_CHUNKS, DIM], F32R)
        one_hot = sb("one_hot", [P, HOT_RING, MAX_CHUNKS, COLS], F32R)
        row_id_int = sb("row_id_int", [P, 2, MAX_CHUNKS], I32)
        row_id = sb("row_id", [P, 2, MAX_CHUNKS])
        ident = sb("ident", [P, P])
        et = sb("et", [P, COLS, FEATURES])
        w1_sb = sb("w1_sb", [P, len(K1), HIDDEN1])
        w2_sb = sb("w2_sb", [P, K2, HIDDEN2])
        vectors = sb("vectors", [P, K2 + 2 * M2])
        b1_sb, b2_sb, w3_sb = vectors[:, 0:K2], vectors[:, K2:K2 + M2], vectors[:, K2 + M2:K2 + 2 * M2]
        y_sb = sb("y_sb", [P, TILES])
        work = sb("work", [P, 2 * SIDE + K2 + M2, COLS])
        low_cols, zt = work[:, 0:SIDE, :], work[:, SIDE:2 * SIDE, :]
        h1, h2 = work[:, 2 * SIDE:2 * SIDE + K2, :], work[:, 2 * SIDE + K2:, :]
        work_flat = work[:, :, :].rearrange("p a b -> p (a b)")
        raw = [work_flat[:, s * MAX_CHUNKS * DIM:(s + 1) * MAX_CHUNKS * DIM] for s in range(2)]

        fill_ps = [ctx.enter_context(nc.psum_tensor(f"fill_ps{i}", [P, 512], F32)) for i in range(FILL_RING)]
        pair_ps = [ctx.enter_context(nc.psum_tensor(f"pair_ps{i}", [P, 512], F32)) for i in range(2)]
        mlp_ps = [ctx.enter_context(nc.psum_tensor(f"mlp_ps{i}", [P, 512], F32)) for i in range(2)]

        ids_in = sem("ids_in")
        index_ok = sem("index_ok")
        rows_in = [sem(f"rows_in{s}") for s in range(GROUP_TILES)]
        gather_tick = sem("gather_tick")
        hot_ids_in = [sem(f"hot_ids_in{k}") for k in range(N_HOT)]
        raw_in = [sem(f"raw_in{s}") for s in range(2)]
        hi_made = sem("hi_made")
        lo_made = sem("lo_made")
        hot_made = sem("hot_made")
        hot_used = sem("hot_used")
        consts = sem("consts")
        row_id_ok = sem("row_id_ok")
        cold_full = sem("cold_full")
        fill_moved = sem("fill_moved")
        pair_full = sem("pair_full")
        pair_moved_v = sem("pair_moved_v")
        pair_moved_a = sem("pair_moved_a")
        zt_clear = sem("zt_clear")
        z_in = sem("z_in")
        w_in = sem("w_in")
        h1_full = sem("h1_full")
        h1_done = sem("h1_done")
        h2_full = sem("h2_full")
        h2_done = sem("h2_done")
        y_full = sem("y_full")
        y_done = sem("y_done")
        stored = sem("stored")

        N_W = 3
        block = ctx.enter_context(nc.Block())

        def periods(engine, period):
            period(0, 0)
            period(0, 1)
            with engine.Fori(1, GROUPS // 2) as turn:
                period(turn, 0)
                period(turn, 1)

        def steps(turn, h):
            n = 0
            for kind, j in FIRST_ORDER if is_first(turn, h) else ORDER_OF_STEPS:
                yield (kind, j), n
                n += {"hot": 1, "tile": N_TF, "layer": 0}[kind]

        def is_first(turn, h):
            return isinstance(turn, int) and turn == 0 and h == 0

        def mlp_psum(m):
            return mlp_ps[m // 2][:, (m % 2) * COLS:(m % 2 + 1) * COLS]

        def load_hot_ids(engine, i):
            for k in range(N_HOT):
                engine.dma_start(hot_ids[0:HOT_ROWS, k, :],
                                 ids_hot[k:k + 1, bass.ds(i * COLS, COLS)].to_broadcast([HOT_ROWS, COLS])
                                 ).then_inc(hot_ids_in[k], 16)

        def move_pairs(engine, i, strips, moved, copy):
            to = work[:, 0:2 * SIDE, :].rearrange("p (half c) b -> p half c b", half=2)
            for bank in range(PAIR_BANKS):
                engine.wait_ge(pair_full, i * PAIR_BANKS + bank + 1)
                for s in strips:
                    frm = pair_ps[bank % 2][32 * s:32 * s + PAIR_COLS, 0:BANK_ROWS * PAIR_COLS].rearrange(
                        "p (r half g) -> p half g r", r=BANK_ROWS, half=2)
                    at = s * STRIP + bank * BANK_ROWS
                    for q in range(STRIPS):
                        n = len(range(q, HALF, STRIPS))
                        last = copy(to[32 * q:32 * q + PAIR_COLS, :, 0:n, at:at + BANK_ROWS],
                                    frm[:, :, q:HALF:STRIPS, :])
                last.then_inc(moved, 1)

        @block.sync
        def _(sp):
            sp.dma_start(ids_sb[:, :], ids.rearrange("(p t) f -> p (t f)", t=TILES)).then_inc(ids_in, 16)
            for k, f in enumerate(HOT):
                wait_count(sp, lo_made, k - 1)
                sp.dma_start(raw[k % 2][0:HOT_ROWS, 0:HOT_CHUNKS[k] * DIM],
                             tables[f].rearrange("(p c) d -> p (c d)", p=HOT_ROWS)).then_inc(raw_in[k % 2], 16)

            def period(turn, h):
                i = 2 * turn + h
                if is_first(turn, h):
                    sp.wait_ge(zt_clear, 1)
                wait_count(sp, h1_full, i)
                sp.dma_start(zt[32:32 + DENSE, SIDE - 1, :], dense[:, bass.ds(i * COLS, COLS)]).then_inc(z_in, 16)
                sp.wait_ge(pair_moved_v, (i + 1) * PAIR_BANKS)
                sp.wait_ge(pair_moved_a, (i + 1) * PAIR_BANKS)
                for low in range(1, HALF + 1):
                    (q0, c0), (q1, c1) = place(low), place(FEATURES - low)
                    sp.dma_start(zt[32 * q1 + FEATURES - low:32 * q1 + FEATURES, c1, :],
                                 low_cols[32 * q0:32 * q0 + low, c0, :]).then_inc(z_in, 16)

            periods(sp, period)
            sp.wait_ge(y_done, GROUPS)
            sp.dma_start(out.rearrange("(p t) o -> p (t o)", t=TILES), y_sb[:, :]).then_inc(stored, 16)
            sp.wait_ge(stored, 16)

        @block.gpsimd
        def _(pool):
            nc.gpsimd.memset(ident[:, :], 0.0).then_inc(consts, 1)
            nc.gpsimd.iota(row_id_int[:, 0, :], pattern=[[1, MAX_CHUNKS]], base=0,
                           channel_multiplier=min(HOT_CHUNKS)).then_inc(consts, 1)
            nc.gpsimd.iota(row_id_int[:, 1, :], pattern=[[1, MAX_CHUNKS]], base=0,
                           channel_multiplier=MAX_CHUNKS).then_inc(consts, 1)
            pool.wait_ge(consts, 3)
            nc.gpsimd.affine_select(out=ident[:, :], in_=ident[:, :], compare_op=ALU.not_equal, fill=1.0, base=0,
                                    pattern=[[-1, P]], channel_multiplier=1).then_inc(consts, 1)
            pool.wait_ge(ids_in, 16)

            def period(turn, h):
                for t in range(GROUP_TILES):
                    i = 2 * turn + h
                    tile = i * GROUP_TILES + t
                    if not is_first(turn, h):
                        pool.wait_ge(cold_full, (i - 1) * (GROUP_TILES * N_TF) + (t + 1) * N_TF)
                    if not isinstance(turn, int):
                        pool.sem_inc(gather_tick, 1)
                    nc.gpsimd.tensor_copy(index[:, t, :], ids_sb[:, bass.ds(tile * FEATURES, FEATURES)]
                                          ).then_inc(index_ok, 1)
                    pool.wait_ge(index_ok, tile + 1)
                    if not isinstance(turn, int):
                        pool.sem_inc(gather_tick, 1)
                    for c, f in enumerate(COLD):
                        nc.gpsimd.indirect_dma_start(
                            out=rows[:, t, c, :], out_offset=None, in_=tables[f],
                            in_offset=bass.IndirectOffsetOnAxis(ap=index[:, t, f:f + 1].bitcast(U32), axis=0),
                        ).then_inc(rows_in[t], 16)

            periods(pool, period)

        @block.tensor
        def _(pe):
            def fill_bank(turn, h, n):
                wait_count(pe, fill_moved, (2 * turn + h) * FILLS + n + 1 - FILL_RING)
                return fill_ps[(h * FILLS + n) % FILL_RING]

            def transpose_tile(turn, h, n0, t):
                pe.wait_ge(rows_in[t], (2 * turn + h + 1) * (16 * N_COLD))
                for j, (c0, n) in enumerate(TILE_FILLS):
                    bank = fill_bank(turn, h, n0 + j)
                    for c in range(n):
                        last = nc.tensor.transpose(bank[:, c * P:(c + 1) * P], rows[:, t, c0 + c, :], ident[:, :])
                    last.then_inc(cold_full, 1)

            def look_up(turn, h, n0, j):
                k0, n = HOT_FILLS[j]
                bank = fill_bank(turn, h, n0)
                for k in range(k0, k0 + n):
                    if is_first(turn, h):
                        pe.wait_ge(hi_made, k + 1)
                        pe.wait_ge(lo_made, k + 1)
                    pe.wait_ge(hot_made, (2 * turn + h) * N_HOT + k + 1)
                    to = bank[:, (k - k0) * COLS:(k - k0 + 1) * COLS]
                    for c in range(HOT_CHUNKS[k]):
                        hot = one_hot[0:HOT_ROWS, (h * N_HOT + k) % HOT_RING, c, :]
                        nc.tensor.matmul(to, table_hi[0:HOT_ROWS, CHUNK_AT[k] + c, :], hot,
                                         start=(c == 0), stop=False)
                        last = nc.tensor.matmul(to, table_lo[0:HOT_ROWS, CHUNK_AT[k] + c, :], hot,
                                                start=False, stop=(c == HOT_CHUNKS[k] - 1))
                    last.then_inc(hot_used, 1)

            def layer1(i):
                pe.wait_ge(z_in, (i + 1) * (16 * MOVES))
                wait_count(pe, y_done, i)
                for m in range(K2):
                    for c, k in enumerate(K1):
                        last = nc.tensor.matmul(mlp_psum(m), w1_sb[0:k, c, m * P:(m + 1) * P], zt[0:k, c, :],
                                                start=(c == 0), stop=(c == len(K1) - 1))
                last.then_inc(h1_full, 1)

            def layer2(i):
                pe.wait_ge(h1_done, (i + 1) * K2)
                for m in range(M2):
                    for c in range(K2):
                        last = nc.tensor.matmul(mlp_psum(m), w2_sb[:, c, m * P:(m + 1) * P], h1[:, c, :],
                                                start=(c == 0), stop=(c == K2 - 1))
                last.then_inc(h2_full, 1)

            def layer3(i):
                pe.wait_ge(h2_done, (i + 1) * M2)
                for t in range(GROUP_TILES):
                    for c in range(M2):
                        last = nc.tensor.matmul(mlp_ps[1][:, t:t + 1], h2[:, c, t * P:(t + 1) * P],
                                                w3_sb[:, c:c + 1], start=(c == 0), stop=(c == M2 - 1))
                last.then_inc(y_full, 1)

            def all_pairs(i):
                pe.wait_ge(fill_moved, (i + 1) * FILLS)
                for bank in range(PAIR_BANKS):
                    wait_count(pe, pair_moved_v, i * PAIR_BANKS + bank - 1)
                    wait_count(pe, pair_moved_a, i * PAIR_BANKS + bank - 1)
                    for r in range(BANK_ROWS):
                        for strip in range(STRIPS):
                            row = strip * STRIP + bank * BANK_ROWS + r
                            last = nc.tensor.matmul(
                                pair_ps[bank % 2][32 * strip:32 * strip + PAIR_COLS, r * PAIR_COLS:(r + 1) * PAIR_COLS],
                                et[:, row, 0:FEATURES - 1], et[:, row, 1:FEATURES], start=True, stop=True)
                    last.then_inc(pair_full, 1)

            def period(turn, h):
                i = 2 * turn + h
                for (kind, j), n0 in steps(turn, h):
                    if kind == "hot":
                        look_up(turn, h, n0, j)
                    elif kind == "tile":
                        transpose_tile(turn, h, n0, j)
                    else:
                        (layer1, layer2, layer3)[j - 1](i - 1)
                all_pairs(i)

            pe.wait_ge(consts, 4)
            pe.wait_ge(w_in, 16 * N_W)
            periods(pe, period)
            layer1(GROUPS - 1)
            layer2(GROUPS - 1)
            layer3(GROUPS - 1)

        @block.scalar
        def _(act):
            load_hot_ids(act, 0)
            act.dma_start(w1_sb[:, :, :], w1.rearrange("(c p) n -> p c n", p=P)).then_inc(w_in, 16)
            act.dma_start(w2_sb[:, :, :], w2.rearrange("(c p) n -> p c n", p=P)).then_inc(w_in, 16)
            act.dma_start(vectors[:, :], vectors_dram).then_inc(w_in, 16)

            def bank(h, n):
                return fill_ps[(h * FILLS + n) % FILL_RING]

            def move_tile(turn, h, n0, t):
                for j, (c0, n) in enumerate(TILE_FILLS):
                    act.wait_ge(cold_full, (2 * turn + h) * (GROUP_TILES * N_TF) + t * N_TF + j + 1)
                    nc.scalar.copy(et[:, t * P:(t + 1) * P, c0:c0 + n].rearrange("p r f -> p f r"),
                                   bank(h, n0 + j)[:, 0:n * P].rearrange("p (f r) -> p f r", f=n)
                                   ).then_inc(fill_moved, 1)

            def move_hot(turn, h, n0, j):
                k0, n = HOT_FILLS[j]
                act.wait_ge(hot_used, (2 * turn + h) * N_HOT + k0 + n)
                nc.scalar.copy(et[:, :, N_COLD + k0:N_COLD + k0 + n].rearrange("p r f -> p f r"),
                               bank(h, n0)[:, 0:n * COLS].rearrange("p (f r) -> p f r", f=n)
                               ).then_inc(fill_moved, 1)

            def relu1(i):
                act.wait_ge(h1_full, i + 1)
                for m in range(K2):
                    nc.scalar.activation(h1[:, m, :], mlp_psum(m), ACT.Relu,
                                         bias=b1_sb[:, m:m + 1]).then_inc(h1_done, 1)

            def relu2(i):
                act.wait_ge(h2_full, i + 1)
                for m in range(M2):
                    nc.scalar.activation(h2[:, m, :], mlp_psum(m), ACT.Relu,
                                         bias=b2_sb[:, m:m + 1]).then_inc(h2_done, 1)

            def period(turn, h):
                i = 2 * turn + h
                for (kind, j), n0 in steps(turn, h):
                    if kind == "hot":
                        move_hot(turn, h, n0, j)
                    elif kind == "tile":
                        move_tile(turn, h, n0, j)
                    elif j < 3:
                        (relu1, relu2)[j - 1](i - 1)
                act.wait_ge(hot_made, (i + 1) * N_HOT)
                load_hot_ids(act, i + 1)
                if is_first(turn, h):
                    act.wait_ge(zt_clear, 1)
                move_pairs(act, i, (2, 3), pair_moved_a, nc.scalar.copy)

            act.wait_ge(w_in, 16 * N_W)
            periods(act, period)
            relu1(GROUPS - 1)
            relu2(GROUPS - 1)

        @block.vector
        def _(dve):
            dve.wait_ge(consts, 3)
            nc.vector.tensor_copy(row_id[:, :, :], row_id_int[:, :, :]).then_inc(row_id_ok, 1)
            dve.wait_ge(row_id_ok, 1)

            def cut_table(k):
                c0, c1 = CHUNK_AT[k], CHUNK_AT[k] + HOT_CHUNKS[k]
                dve.wait_ge(raw_in[k % 2], 16 * (k // 2 + 1))
                src = raw[k % 2][0:HOT_ROWS, 0:HOT_CHUNKS[k] * DIM].rearrange("p (c d) -> p c d", d=DIM)
                nc.vector.tensor_copy(table_hi[0:HOT_ROWS, c0:c1, :], src).then_inc(hi_made, 1)
                dve.wait_ge(hi_made, k + 1)
                nc.vector.tensor_tensor(table_lo[0:HOT_ROWS, c0:c1, :], src,
                                        table_hi[0:HOT_ROWS, c0:c1, :].bitcast(F32), ALU.subtract
                                        ).then_inc(lo_made, 1)

            def make_one_hot(turn, h, k):
                n = (2 * turn + h) * N_HOT + k
                dve.wait_ge(hot_ids_in[k], (2 * turn + h + 1) * 16)
                wait_count(dve, hot_used, n + 1 - HOT_RING)
                which = 0 if HOT_CHUNKS[k] == min(HOT_CHUNKS) else 1
                for c in range(HOT_CHUNKS[k]):
                    last = nc.vector.tensor_scalar(one_hot[0:HOT_ROWS, (h * N_HOT + k) % HOT_RING, c, :],
                                                   hot_ids[0:HOT_ROWS, k, :],
                                                   row_id[0:HOT_ROWS, which, c:c + 1], None, ALU.is_equal)
                last.then_inc(hot_made, 1)

            def output(i):
                dve.wait_ge(y_full, i + 1)
                nc.vector.tensor_scalar(y_sb[:, bass.ds(i * GROUP_TILES, GROUP_TILES)], mlp_ps[1][:, 0:GROUP_TILES],
                                        1.0, None, ALU.mult).then_inc(y_done, 1)

            def period(turn, h):
                i = 2 * turn + h
                for k in range(N_HOT):
                    if is_first(turn, h):
                        cut_table(k)
                    make_one_hot(turn, h, k)
                if not is_first(turn, h):
                    output(i - 1)
                if is_first(turn, h):
                    dve.wait_ge(lo_made, N_HOT)
                    nc.vector.memset(zt, 0.0).then_inc(zt_clear, 1)
                    dve.wait_ge(zt_clear, 1)
                move_pairs(dve, i, (0, 1), pair_moved_v, nc.vector.tensor_copy)

            periods(dve, period)
            output(GROUPS - 1)
            for k in range(N_HOT):
                dve.wait_ge(hot_ids_in[k], (GROUPS + 1) * 16)


def kernel(**inputs):
    import concourse.bacc as bacc
    from concourse.bass_utils import run_bass_kernel_spmd

    nc = bacc.Bacc("TRN2", target_bir_lowering=False, num_devices=1)
    arrays = {}

    def dram(name, array):
        array = np.ascontiguousarray(array)
        arrays[name] = array
        return nc.dram_tensor(name, array.shape, mybir.dt.from_np(array.dtype), kind="ExternalInput").ap()

    def by_tile(columns):
        n = columns.shape[1]
        return columns.reshape(P, TILES, n).transpose(2, 1, 0).reshape(n, BATCH)

    ids_np = np.asarray(inputs["ids"])
    hot_np = by_tile(ids_np[:, HOT])
    hot_np = np.concatenate([hot_np, hot_np[:, :COLS]], axis=1)
    ids = dram("ids_d", ids_np)
    ids_hot = dram("ids_hot_d", hot_np)
    tables = [dram(f"tbl_{f}_d", inputs[f"tbl_{f}"]) for f in range(FEATURES)]
    dense = dram("dense_d", by_tile(np.asarray(inputs["dense_ctx"])))
    w1_np = np.zeros((SIDE * P, HIDDEN1), np.float32)
    for row, source in enumerate(contraction_rows()):
        if source is not None:
            w1_np[row] = inputs["W_top1"][source]
    w1 = dram("w1_d", w1_np)
    w2 = dram("w2_d", inputs["W_top2"])
    vectors = dram("vectors_d", np.concatenate(
        [np.asarray(inputs[name]).reshape(-1, P).T for name in ("b_top1", "b_top2", "W_top3")], axis=1))
    out = nc.dram_tensor("out_d", (BATCH, 1), F32, kind="ExternalOutput").ap()
    build(nc, ids, ids_hot, tables, dense, w1, w2, vectors, out)
    result = run_bass_kernel_spmd(nc, [arrays], core_ids=[0])
    return result.results[0]["out_d"]
```

```python
from contextlib import ExitStack

import numpy as np

import concourse.bass as bass
from concourse import mybir

F32 = mybir.dt.float32
F32R = mybir.dt.float32r
I32 = mybir.dt.int32
U32 = mybir.dt.uint32
ALU = mybir.AluOpType
ACT = mybir.ActivationFunctionType

P = 128
BATCH = 2048
FEATURES = 27
DIM = 128
DENSE = 16
VOCAB = [1250, 125000, 12500, 1000, 1250, 1000, 1250, 1250, 1250, 1250, 12500, 1250, 1250, 1250,
         12500, 12500, 12500, 1000, 12500, 12500, 1250, 1000, 12500, 1250, 1000, 1250, 1250]
HIDDEN1, HIDDEN2 = 512, 256

N_HOT = 9
EARLY_HOT = (9, 9)
LATE_HOT = (8, 9)
HOT = sorted(range(FEATURES), key=lambda f: (VOCAB[f], f))[:N_HOT]
N_SWING = N_HOT - min(EARLY_HOT + LATE_HOT)
COLD = [f for f in range(FEATURES) if f not in HOT] + HOT[N_HOT - N_SWING:]
N_COLD = len(COLD)
ORDER = COLD + HOT[:N_HOT - N_SWING]
HOT_ROWS = 125
HOT_CHUNKS = [VOCAB[f] // HOT_ROWS for f in HOT]
MAX_CHUNKS = max(HOT_CHUNKS)
CHUNK_AT = [sum(HOT_CHUNKS[:k]) for k in range(N_HOT)]
ALL_CHUNKS = sum(HOT_CHUNKS)

TILES = BATCH // P
GROUP_TILES = 2
COLS = GROUP_TILES * P
GROUPS = TILES // GROUP_TILES
HOT_RING = 3

STRIPS = 4
STRIP = P // STRIPS
PAIR_COLS = FEATURES - 1
BANK_ROWS = 16
PAIR_BANKS = COLS // (STRIPS * BANK_ROWS)
TILE_BANKS = PAIR_BANKS // GROUP_TILES

TILE_FILLS = [(c, min(4, N_COLD - c)) for c in range(0, N_COLD, 4)]
HOT_FILLS = [(k, min(2, N_HOT - k)) for k in range(0, N_HOT, 2)]
N_TF, N_HF = len(TILE_FILLS), len(HOT_FILLS)
FILL_RING = 4
RAW_SLOTS = 4


def cold_count(n_hot):
    return FEATURES - n_hot


def tile_fills(n_hot):
    return [(c, min(n, cold_count(n_hot) - c)) for c, n in TILE_FILLS]


def hot_fills(n_hot):
    return HOT_FILLS[:-(-n_hot // 2)]


def fills(n_hot):
    return GROUP_TILES * N_TF + len(hot_fills(n_hot))


def order(first, last, n_hot):
    hot = [("hot", j) for j in range(len(hot_fills(n_hot)))]
    if first:
        return (hot[:3] + [("tile", 0)] + hot[3:]
                + [("pairs", 0), ("pairs", 1), ("tile", 1), ("pairs", 2), ("pairs", 3)])
    start = (hot[:4] + [("tile", 0)] + hot[4:]
             + [("layer", 1), ("pairs", 0), ("layer", 2), ("tile", 1), ("pairs", 1)])
    if last:
        return start + [("pairs", 2), ("pairs", 3), ("layer", 3)]
    return start + [("layer", 3), ("pairs", 2), ("pairs", 3)]


WARM = 10
AHEAD = 3

PAIRS = FEATURES * (FEATURES - 1) // 2
CHUNKS = -(-(PAIRS + DENSE) // P)
HIGH = FEATURES - STRIPS * CHUNKS
LOW_SLOTS = -(-(HIGH - 1) // STRIPS)
SLOTS = LOW_SLOTS + CHUNKS
K2 = HIDDEN1 // P
M2 = HIDDEN2 // P
MOVES = HIGH - 1


def place(i):
    strip = (i - 1) % STRIPS
    return strip, SLOTS - len(range(strip, PAIR_COLS, STRIPS)) + (i - 1) // STRIPS


def homes():
    filled = {i: i for i in range(HIGH, FEATURES)}
    found = {}

    def put(name, n, high):
        strip, slot = place(high)
        found[name] = strip, slot - LOW_SLOTS, filled[high]
        filled[high] += n

    put(0, DENSE, STRIP - DENSE)
    for low in reversed(range(1, HIGH)):
        put(low, low, min(filled, key=lambda i: (filled[i], i)))
    assert all(PAIR_COLS <= n <= STRIP for n in filled.values())
    return found


HOMES = homes()
ALL_LOWS = list(range(1, HIGH)) + [0]


def lows_of(chunk):
    return [low for low in ALL_LOWS if HOMES[low][1] == chunk]


LAST_ORDER = [2, 1, 0]
POOL_LAST_0, SP_LAST_0 = lows_of(0)[:2], lows_of(0)[2:]


def contraction_rows():
    def pair(i, j):
        hi, lo = max(ORDER[i], ORDER[j]), min(ORDER[i], ORDER[j])
        return hi * (hi - 1) // 2 + lo

    rows = [None] * (CHUNKS * P)
    for i in range(1, FEATURES):
        if i < HIGH:
            strip, chunk, first = HOMES[i]
        else:
            strip, chunk, first = place(i)[0], place(i)[1] - LOW_SLOTS, 0
        at = chunk * P + STRIP * strip + first
        rows[at:at + i] = [pair(i, j) for j in range(i)]
    strip, chunk, first = HOMES[0]
    at = chunk * P + STRIP * strip + first
    rows[at:at + DENSE] = range(PAIRS, PAIRS + DENSE)
    return rows


def wait_count(engine, semaphore, count):
    if not isinstance(count, int) or count > 0:
        engine.wait_ge(semaphore, count)


def build(nc, ids, ids_hot, tables, dense, w1, w2, vectors_dram, out):
    with ExitStack() as ctx:
        def sb(name, shape, dtype=F32):
            return ctx.enter_context(nc.sbuf_tensor(name, shape, dtype))

        def sem(name):
            return ctx.enter_context(nc.semaphore(name))

        ids_sb = sb("ids_sb", [P, TILES * FEATURES], I32)
        index = sb("index", [P, 2, GROUP_TILES * FEATURES], I32)
        rows = sb("rows", [P, GROUP_TILES, N_COLD, DIM])
        hot_ids = sb("hot_ids", [P, 2, N_HOT, COLS], I32)
        table_hi = sb("table_hi", [P, ALL_CHUNKS, DIM], F32R)
        table_lo = sb("table_lo", [P, ALL_CHUNKS, DIM], F32R)
        one_hot = sb("one_hot", [P, HOT_RING, MAX_CHUNKS, COLS], F32R)
        first_row_int = sb("first_row_int", [P, 2], I32)
        first_row = sb("first_row", [P, 2])
        ident = sb("ident", [P, P])
        et = sb("et", [P, COLS, FEATURES])
        w1_sb = sb("w1_sb", [P, CHUNKS, HIDDEN1])
        w2_sb = sb("w2_sb", [P, K2, HIDDEN2])
        vectors = sb("vectors", [P, K2 + 2 * M2])
        b1_sb, b2_sb, w3_sb = vectors[:, 0:K2], vectors[:, K2:K2 + M2], vectors[:, K2 + M2:K2 + 2 * M2]
        y_row = sb("y_row", [1, COLS])
        work = sb("work", [P, max(SLOTS + K2 + M2, (RAW_SLOTS - 1) * MAX_CHUNKS * DIM // COLS), COLS])
        pair_cols = work[:, 0:SLOTS, :]
        low_cols, zt = work[:, 0:LOW_SLOTS, :], work[:, LOW_SLOTS:SLOTS, :]
        h1, h2 = work[:, SLOTS:SLOTS + K2, :], work[:, SLOTS + K2:SLOTS + K2 + M2, :]
        work_flat = work[:, :, :].rearrange("p a b -> p (a b)")
        raw = [work_flat[:, s * MAX_CHUNKS * DIM:(s + 1) * MAX_CHUNKS * DIM] for s in range(RAW_SLOTS - 1)]
        raw.append(w1_sb[:, :, :].rearrange("p a b -> p (a b)"))

        fill_ps = [ctx.enter_context(nc.psum_tensor(f"fill_ps{i}", [P, 512], F32)) for i in range(FILL_RING)]
        pair_ps = [ctx.enter_context(nc.psum_tensor(f"pair_ps{i}", [P, 512], F32)) for i in range(2)]
        mlp_ps = [ctx.enter_context(nc.psum_tensor(f"mlp_ps{i}", [P, 512], F32)) for i in range(2)]
        y_ps = mlp_ps[0][0:1, COLS:2 * COLS]

        ids_in = sem("ids_in")
        index_ok = sem("index_ok")
        rows_in = [sem(f"rows_in{s}") for s in range(GROUP_TILES)]
        gather_tick = sem("gather_tick")
        hot_ids_in = [sem(f"hot_ids_in{k}") for k in range(2)]
        raw_in = [sem(f"raw_in{s}") for s in range(RAW_SLOTS)]
        hi_made = sem("hi_made")
        lo_made = sem("lo_made")
        hot_made = sem("hot_made")
        hot_used = sem("hot_used")
        consts = sem("consts")
        first_row_ok = sem("first_row_ok")
        hot_ids_local = sem("hot_ids_local")
        cold_full = sem("cold_full")
        fill_moved = sem("fill_moved")
        pair_full = sem("pair_full")
        pair_moved_v = sem("pair_moved_v")
        pair_moved_a = sem("pair_moved_a")
        zt_clear = sem("zt_clear")
        z_in = sem("z_in")
        z_last_in = [sem(f"z_last_in{c}") for c in range(CHUNKS)]
        dense_in = sem("dense_in")
        w_in = sem("w_in")
        h1_full = sem("h1_full")
        h1_done = sem("h1_done")
        h2_full = sem("h2_full")
        h2_done = sem("h2_done")
        y_full = sem("y_full")
        y_done = sem("y_done")
        stored = sem("stored")

        N_W = 3
        block = ctx.enter_context(nc.Block())

        def periods(engine, period, peeled=1):
            period(0, 0)
            period(0, 1)
            with engine.Fori(1, GROUPS // 2 - peeled) as turn:
                period(turn, 0)
                period(turn, 1)
            for turn in range(GROUPS // 2 - peeled, GROUPS // 2):
                period(turn, 0)
                period(turn, 1)

        def complete_zt(engine, i, at, lows, landed):
            engine.wait_ge(pair_moved_v, (i + 1) * PAIR_BANKS)
            engine.wait_ge(pair_moved_a, (i + 1) * PAIR_BANKS)
            for low in lows:
                strip, chunk, first = HOMES[low]
                row = STRIP * strip + first
                if low == 0:
                    engine.dma_start(zt[row:row + DENSE, chunk, :], dense[:, bass.ds(at, COLS)]).then_inc(dense_in, 16)
                else:
                    from_row, slot = STRIP * place(low)[0], place(low)[1]
                    engine.dma_start(zt[row:row + low, chunk, :],
                                     low_cols[from_row:from_row + low, slot, :]).then_inc(landed, 16)

        def steps(turn, h):
            n = 0
            for kind, j in order(is_first(turn, h), is_last(2 * turn + h), n_hot(turn, h)):
                yield (kind, j), n
                n += {"hot": 1, "tile": N_TF}.get(kind, 0)

        def is_last(i):
            return isinstance(i, int) and i == GROUPS - 1

        def is_first(turn, h):
            return isinstance(turn, int) and turn == 0 and h == 0

        def n_hot(turn, h):
            return (EARLY_HOT if isinstance(turn, int) and turn == 0 else LATE_HOT)[h]

        def before(turn, h, count):
            early, late = [count(n) for n in EARLY_HOT], [count(n) for n in LATE_HOT]
            if isinstance(turn, int) and turn == 0:
                return sum(early[:h])
            return turn * sum(late) + (sum(early) - sum(late) + sum(late[:h]))

        def looked_up(n):
            return n

        def mlp_psum(m):
            return mlp_ps[m // 2][:, (m % 2) * COLS:(m % 2 + 1) * COLS]

        def raw_table(k):
            return raw[k % RAW_SLOTS][0:HOT_ROWS, 0:HOT_CHUNKS[k] * DIM].rearrange("p (c d) -> p c d", d=DIM)

        def load_hot_ids(engine, i, h):
            engine.dma_start(hot_ids[0:HOT_ROWS, h, :, :],
                             ids_hot[:, bass.ds(i * COLS, COLS)].partition_broadcast(HOT_ROWS)
                             ).then_inc(hot_ids_in[h], 16)

        def move_pairs(engine, i, bank, strips, moved, copy):
            engine.wait_ge(pair_full, i * PAIR_BANKS + bank + 1)
            for s in strips:
                frm = pair_ps[bank % 2][STRIP * s:STRIP * s + PAIR_COLS, 0:BANK_ROWS * PAIR_COLS].rearrange(
                    "p (r g) -> p g r", r=BANK_ROWS)
                at = bank // TILE_BANKS * P + s * STRIP + bank % TILE_BANKS * BANK_ROWS
                for q in range(STRIPS):
                    last = copy(pair_cols[STRIP * q:STRIP * q + PAIR_COLS, place(q + 1)[1]:, at:at + BANK_ROWS],
                                frm[:, q::STRIPS, :])
            last.then_inc(moved, 1)

        @block.sync
        def _(sp):
            sp.dma_start(ids_sb[:, :], ids).then_inc(ids_in, 16)
            for k, f in enumerate(HOT):
                wait_count(sp, lo_made, k - RAW_SLOTS + 1)
                sp.dma_start(raw[k % RAW_SLOTS][0:HOT_ROWS, 0:HOT_CHUNKS[k] * DIM],
                             tables[f].rearrange("(p c) d -> p (c d)", p=HOT_ROWS)).then_inc(raw_in[k % RAW_SLOTS], 16)

            def period(turn, h):
                i = 2 * turn + h
                at, last_at = i * COLS, i * COLS - COLS
                if not isinstance(turn, int):
                    at, last_at = sp.snap(at), sp.snap(last_at)
                if is_last(i):
                    complete_zt(sp, i, at, lows_of(2), z_last_in[2])
                    complete_zt(sp, i, at, SP_LAST_0, z_in)
                    store(i - 1, last_at)
                else:
                    if not is_first(turn, h):
                        store(i - 1, last_at)
                    complete_zt(sp, i, at, ALL_LOWS, z_in)

            def store(i, at):
                sp.wait_ge(y_done, i + 1)
                sp.dma_start(out[0:1, bass.ds(at, COLS)], y_row[0:1, :]).then_inc(stored, 16)

            periods(sp, period)
            store(GROUPS - 1, (GROUPS - 1) * COLS)
            sp.wait_ge(stored, 16 * GROUPS)

        @block.gpsimd
        def _(pool):
            nc.gpsimd.memset(ident[:, :], 0.0).then_inc(consts, 1)
            for n, chunks in enumerate((min(HOT_CHUNKS), MAX_CHUNKS)):
                nc.gpsimd.iota(first_row_int[:, n:n + 1], pattern=[[0, 1]], base=0,
                               channel_multiplier=chunks).then_inc(consts, 1)
            pool.wait_ge(consts, 3)
            nc.gpsimd.affine_select(out=ident[:, :], in_=ident[:, :], compare_op=ALU.not_equal, fill=1.0, base=0,
                                    pattern=[[-1, P]], channel_multiplier=1).then_inc(consts, 1)
            pool.wait_ge(ids_in, 16)

            def period(turn, h):
                for t in range(GROUP_TILES):
                    i = 2 * turn + h
                    tile = i * GROUP_TILES + t
                    if not is_first(turn, h):
                        pool.wait_ge(cold_full, (i - 1) * (GROUP_TILES * N_TF) + (t + 1) * N_TF)
                    if isinstance(turn, int):
                        numbers = ids_sb[:, tile * FEATURES:(tile + 1) * FEATURES]
                    else:
                        if t == 0:
                            pool.wait_ge(index_ok, i - 1)
                        pool.sem_inc(gather_tick, 1)
                        numbers = index[:, h, t * FEATURES:(t + 1) * FEATURES]
                    for c, f in enumerate(COLD[:cold_count(n_hot(turn, h))]):
                        nc.gpsimd.indirect_dma_start(
                            out=rows[:, t, c, :], out_offset=None, in_=tables[f],
                            in_offset=bass.IndirectOffsetOnAxis(ap=numbers[:, f:f + 1].bitcast(U32), axis=0),
                        ).then_inc(rows_in[t], 16)

            periods(pool, period, peeled=0)
            complete_zt(pool, GROUPS - 1, (GROUPS - 1) * COLS, lows_of(1), z_last_in[1])
            complete_zt(pool, GROUPS - 1, (GROUPS - 1) * COLS, POOL_LAST_0, z_last_in[0])

        @block.tensor
        def _(pe):
            def fill_bank(turn, h, n):
                wait_count(pe, fill_moved, before(turn, h, fills) + max(n + 1 - FILL_RING, 0))
                return fill_ps[n % FILL_RING]

            def transpose_tile(turn, h, n0, t):
                landed = before(turn, h, lambda n: 16 * cold_count(n)) + 16 * cold_count(n_hot(turn, h))
                pe.wait_ge(rows_in[t], landed)
                for j, (c0, n) in enumerate(tile_fills(n_hot(turn, h))):
                    bank = fill_bank(turn, h, n0 + j)
                    for c in range(n):
                        last = nc.tensor.transpose(bank[:, c * P:(c + 1) * P], rows[:, t, c0 + c, :], ident[:, :])
                    last.then_inc(cold_full, 1)

            def look_up(turn, h, n0, j):
                k0, n = HOT_FILLS[j]
                bank = fill_bank(turn, h, n0)
                for k in range(k0, k0 + n):
                    if is_first(turn, h):
                        pe.wait_ge(hi_made, k + 1)
                        pe.wait_ge(lo_made, k + 1)
                    pe.wait_ge(hot_made, before(turn, h, looked_up) + k + 1)
                    to = bank[:, (k - k0) * COLS:(k - k0 + 1) * COLS]
                    for c in range(HOT_CHUNKS[k]):
                        hot = one_hot[0:HOT_ROWS, k % HOT_RING, c, :]
                        nc.tensor.matmul(to, table_hi[0:HOT_ROWS, CHUNK_AT[k] + c, :], hot,
                                         start=(c == 0), stop=False)
                        last = nc.tensor.matmul(to, table_lo[0:HOT_ROWS, CHUNK_AT[k] + c, :], hot,
                                                start=False, stop=(c == HOT_CHUNKS[k] - 1))
                    last.then_inc(hot_used, 1)

            def layer1(i):
                pe.wait_ge(z_in, (i + 1) * (16 * MOVES))
                pe.wait_ge(dense_in, (i + 1) * 16)
                wait_count(pe, y_done, i)
                for m in range(K2):
                    for c in range(CHUNKS):
                        last = nc.tensor.matmul(mlp_psum(m), w1_sb[:, c, m * P:(m + 1) * P], zt[:, c, :],
                                                start=(c == 0), stop=(c == CHUNKS - 1))
                    if m % 2 == 1:
                        last.then_inc(h1_full, 1)

            def layer1_last():
                for c in LAST_ORDER:
                    pe.wait_ge(z_last_in[c], 16 * len(lows_of(c) if c else POOL_LAST_0))
                    if c == 0:
                        pe.wait_ge(z_in, (GROUPS - 1) * (16 * MOVES) + 16 * (len(SP_LAST_0) - 1))
                        pe.wait_ge(dense_in, 16 * GROUPS)
                    for m in range(K2):
                        last = nc.tensor.matmul(fill_ps[m][:, 0:COLS], w1_sb[:, c, m * P:(m + 1) * P], zt[:, c, :],
                                                start=(c == LAST_ORDER[0]), stop=(c == LAST_ORDER[-1]))
                        if c == LAST_ORDER[-1]:
                            last.then_inc(h1_full, 1)

            def layer2(i):
                for m in range(M2):
                    for c in range(K2):
                        if m == 0:
                            done = c if is_last(i) else max(c, 1)
                            pe.wait_ge(h1_done, i * K2 + done + 1)
                        last = nc.tensor.matmul(mlp_ps[m][:, 0:COLS], w2_sb[:, c, m * P:(m + 1) * P], h1[:, c, :],
                                                start=(c == 0), stop=(c == K2 - 1))
                    last.then_inc(h2_full, 1)

            def layer3(i):
                for c in range(M2):
                    pe.wait_ge(h2_done, i * M2 + c + 1)
                    last = nc.tensor.matmul(y_ps, w3_sb[:, c:c + 1], h2[:, c, :],
                                            start=(c == 0), stop=(c == M2 - 1))
                last.then_inc(y_full, 1)

            def row_pairs(turn, h, bank):
                i = 2 * turn + h
                all_moved = before(turn, h, fills) + fills(n_hot(turn, h))
                pe.wait_ge(fill_moved, all_moved - (N_TF if bank < TILE_BANKS else 0))
                wait_count(pe, pair_moved_v, i * PAIR_BANKS + bank - 1)
                wait_count(pe, pair_moved_a, i * PAIR_BANKS + bank - 1)
                for r in range(BANK_ROWS):
                    for s in range(STRIPS):
                        row = bank // TILE_BANKS * P + s * STRIP + bank % TILE_BANKS * BANK_ROWS + r
                        last = nc.tensor.matmul(
                            pair_ps[bank % 2][32 * s:32 * s + PAIR_COLS, r * PAIR_COLS:(r + 1) * PAIR_COLS],
                            et[:, row, 0:FEATURES - 1], et[:, row, 1:FEATURES], start=True, stop=True)
                last.then_inc(pair_full, 1)

            def period(turn, h):
                i = 2 * turn + h
                for (kind, j), n0 in steps(turn, h):
                    if kind == "hot":
                        look_up(turn, h, n0, j)
                    elif kind == "tile":
                        transpose_tile(turn, h, n0, j)
                    elif kind == "pairs":
                        row_pairs(turn, h, j)
                    else:
                        (layer1, layer2, layer3)[j - 1](i - 1)
                if is_first(turn, h):
                    pe.wait_ge(w_in, 16 * N_W)

            pe.wait_ge(consts, 4)
            periods(pe, period)
            for _ in range(WARM):
                nc.tensor.matmul(mlp_ps[1][:, 0:COLS], w2_sb[:, 0, 0:P], h1[:, 0, :], start=True, stop=True)
            layer1_last()
            pe.wait_ge(y_done, GROUPS - 1)
            layer2(GROUPS - 1)
            layer3(GROUPS - 1)

        @block.scalar
        def _(act):
            load_hot_ids(act, 0, 0)

            def load_weights():
                act.wait_ge(lo_made, N_HOT)
                act.dma_start(w1_sb[:, :, :], w1.rearrange("(c p) n -> p c n", p=P)).then_inc(w_in, 16)
                act.dma_start(w2_sb[:, :, :], w2.rearrange("(c p) n -> p c n", p=P)).then_inc(w_in, 16)
                act.dma_start(vectors[:, :], vectors_dram).then_inc(w_in, 16)

            def make_high(k):
                act.wait_ge(raw_in[k % RAW_SLOTS], 16 * (k // RAW_SLOTS + 1))
                nc.scalar.copy(table_hi[0:HOT_ROWS, CHUNK_AT[k]:CHUNK_AT[k] + HOT_CHUNKS[k], :],
                               raw_table(k)).then_inc(hi_made, 1)

            def move_tile(turn, h, n0, t):
                for j, (c0, n) in enumerate(tile_fills(n_hot(turn, h))):
                    act.wait_ge(cold_full, (2 * turn + h) * (GROUP_TILES * N_TF) + t * N_TF + j + 1)
                    nc.scalar.copy(et[:, t * P:(t + 1) * P, c0:c0 + n].rearrange("p r f -> p f r"),
                                   fill_ps[(n0 + j) % FILL_RING][:, 0:n * P].rearrange("p (f r) -> p f r", f=n)
                                   ).then_inc(fill_moved, 1)

            def move_hot(turn, h, n0, j):
                k0, n = HOT_FILLS[j]
                slot = ORDER.index(HOT[k0])
                act.wait_ge(hot_used, before(turn, h, looked_up) + k0 + n)
                nc.scalar.copy(et[:, :, slot:slot + n].rearrange("p r f -> p f r"),
                               fill_ps[n0 % FILL_RING][:, 0:n * COLS].rearrange("p (f r) -> p f r", f=n)
                               ).then_inc(fill_moved, 1)

            def relu1(i):
                last = is_last(i)
                for m in range(K2):
                    act.wait_ge(h1_full, i * (K2 // 2) + (m if last else m // 2) + 1)
                    nc.scalar.activation(h1[:, m, :], fill_ps[m][:, 0:COLS] if last else mlp_psum(m), ACT.Relu,
                                         bias=b1_sb[:, m:m + 1]).then_inc(h1_done, 1)

            def relu2(i):
                for m in range(M2):
                    act.wait_ge(h2_full, i * M2 + m + 1)
                    nc.scalar.activation(h2[:, m, :], mlp_ps[m][:, 0:COLS], ACT.Relu,
                                         bias=b2_sb[:, m:m + 1]).then_inc(h2_done, 1)

            def period(turn, h):
                i = 2 * turn + h
                wait_count(act, hot_made, before(turn, h, looked_up))
                if not is_last(i):
                    load_hot_ids(act, i + 1, 1 - h)
                for (kind, j), n0 in steps(turn, h):
                    if kind == "hot":
                        if is_first(turn, h):
                            for k in range(2 * j + 3, min(2 * j + 5, N_HOT)):
                                make_high(k)
                        move_hot(turn, h, n0, j)
                        if is_first(turn, h) and j == N_HF - 1:
                            load_weights()
                    elif kind == "tile":
                        move_tile(turn, h, n0, j)
                    elif kind == "pairs":
                        if j == 0 and is_first(turn, h):
                            act.wait_ge(zt_clear, 1)
                        if j == 0:
                            wait_count(act, z_in, i * (16 * MOVES))
                        move_pairs(act, i, j, (2, 3), pair_moved_a, nc.scalar.copy)
                    elif j < 3:
                        (relu1, relu2)[j - 1](i - 1)
                if is_first(turn, h):
                    act.wait_ge(w_in, 16 * N_W)

            for k in range(3):
                make_high(k)
            periods(act, period)
            relu1(GROUPS - 1)
            relu2(GROUPS - 1)

        @block.vector
        def _(dve):
            dve.wait_ge(consts, 3)
            dve.wait_ge(ids_in, 16)
            nc.vector.tensor_copy(first_row[:, :], first_row_int[:, :]).then_inc(first_row_ok, 1)
            dve.wait_ge(first_row_ok, 1)

            def make_low(k):
                c0, c1 = CHUNK_AT[k], CHUNK_AT[k] + HOT_CHUNKS[k]
                dve.wait_ge(raw_in[k % RAW_SLOTS], 16 * (k // RAW_SLOTS + 1))
                dve.wait_ge(hi_made, k + 1)
                nc.vector.tensor_tensor(table_lo[0:HOT_ROWS, c0:c1, :], raw_table(k),
                                        table_hi[0:HOT_ROWS, c0:c1, :].bitcast(F32), ALU.subtract
                                        ).then_inc(lo_made, 1)

            def localise_hot_ids(i, h):
                dve.wait_ge(hot_ids_in[h], (i - h) * 8 + 16)
                k = HOT_CHUNKS.count(min(HOT_CHUNKS))
                for n, (k0, k1) in enumerate(((0, k), (k, N_HOT))):
                    ids = hot_ids[0:HOT_ROWS, h, k0:k1, :]
                    nc.vector.tensor_scalar(ids.bitcast(F32), ids, first_row[0:HOT_ROWS, n:n + 1], None, ALU.subtract
                                            ).then_inc(hot_ids_local, 1)
                dve.wait_ge(hot_ids_local, 2 * (i + 1))

            def make_one_hot(made_before, last_n, h, k):
                if k >= HOT_RING:
                    dve.wait_ge(hot_used, made_before + k + 1 - HOT_RING)
                elif last_n:
                    user = max(m for m in range(last_n) if m % HOT_RING == k)
                    dve.wait_ge(hot_used, made_before - last_n + user + 1)
                for c in range(HOT_CHUNKS[k]):
                    last = nc.vector.tensor_scalar(one_hot[0:HOT_ROWS, k % HOT_RING, c, :],
                                                   hot_ids[0:HOT_ROWS, h, k, :].bitcast(F32),
                                                   float(c), None, ALU.is_equal)
                last.then_inc(hot_made, 1)

            def output(i):
                dve.wait_ge(y_full, i + 1)
                nc.vector.tensor_copy(y_row[0:1, :], y_ps).then_inc(y_done, 1)

            def period(turn, h):
                i = 2 * turn + h
                n = n_hot(turn, h)
                made_before = before(turn, h, looked_up)
                if is_first(turn, h):
                    localise_hot_ids(i, h)
                    for k in range(AHEAD):
                        make_one_hot(0, 0, h, k)
                        make_low(k)
                if not is_first(turn, h) and not is_last(i):
                    nc.vector.tensor_copy(index[:, 1 - h, :],
                                          ids_sb[:, bass.ds((i + 1) * (GROUP_TILES * FEATURES), GROUP_TILES * FEATURES)]
                                          ).then_inc(index_ok, 1)
                for k in range(AHEAD, n):
                    if is_first(turn, h):
                        make_low(k)
                    make_one_hot(made_before, None, h, k)
                if is_first(turn, h):
                    dve.wait_ge(lo_made, N_HOT)
                    nc.vector.memset(zt, 0.0).then_inc(zt_clear, 1)
                    dve.wait_ge(zt_clear, 1)
                if not is_last(i):
                    localise_hot_ids(i + 1, 1 - h)
                    for k in range(AHEAD):
                        make_one_hot(made_before + n, n, 1 - h, k)
                wait_count(dve, z_in, i * (16 * MOVES))
                for bank in range(PAIR_BANKS):
                    move_pairs(dve, i, bank, (0, 1), pair_moved_v, nc.vector.tensor_copy)
                    if bank == (PAIR_BANKS - 1 if is_last(i) else 1) and not is_first(turn, h):
                        output(i - 1)
                if not is_first(turn, h):
                    dve.wait_ge(stored, i * 16)

            periods(dve, period)
            output(GROUPS - 1)


def kernel(**inputs):
    import concourse.bacc as bacc
    from concourse.bass_utils import run_bass_kernel_spmd

    nc = bacc.Bacc("TRN2", target_bir_lowering=False, num_devices=1)
    arrays = {}

    def dram(name, array):
        array = np.ascontiguousarray(array)
        arrays[name] = array
        return nc.dram_tensor(name, array.shape, mybir.dt.from_np(array.dtype), kind="ExternalInput").ap()

    def by_tile(columns):
        n = columns.shape[1]
        return columns.reshape(P, TILES, n).transpose(2, 1, 0).reshape(n, BATCH)

    ids_np = np.asarray(inputs["ids"])
    hot_np = by_tile(ids_np[:, HOT])
    ids = dram("ids_d", ids_np.reshape(P, TILES * FEATURES))
    ids_hot = dram("ids_hot_d", hot_np)
    tables = [dram(f"tbl_{f}_d", inputs[f"tbl_{f}"]) for f in range(FEATURES)]
    dense = dram("dense_d", by_tile(np.asarray(inputs["dense_ctx"])))
    w1_np = np.zeros((CHUNKS * P, HIDDEN1), np.float32)
    for row, source in enumerate(contraction_rows()):
        if source is not None:
            w1_np[row] = inputs["W_top1"][source]
    w1 = dram("w1_d", w1_np)
    w2 = dram("w2_d", inputs["W_top2"])
    vectors = dram("vectors_d", np.concatenate(
        [np.asarray(inputs[name]).reshape(-1, P).T for name in ("b_top1", "b_top2", "W_top3")], axis=1))
    out = nc.dram_tensor("out_d", (1, BATCH), F32, kind="ExternalOutput").ap()
    build(nc, ids, ids_hot, tables, dense, w1, w2, vectors, out)
    result = run_bass_kernel_spmd(nc, [arrays], core_ids=[0])
    return np.ascontiguousarray(result.results[0]["out_d"].reshape(TILES, P).T).reshape(BATCH, 1)
```
